# Optimizing a Trainium2 kernel written in Bass

```python
import numpy as np
import jax
import jax.numpy as jnp

def _softmax(x, axis=-1):
    return jax.nn.softmax(x, axis=axis)

def _gelu(x):
    return jax.nn.gelu(x, approximate=True)

def _silu(x):
    return jax.nn.silu(x)

def _sigmoid(x):
    return jax.nn.sigmoid(x)

def _layernorm(x, axis=-1, eps=1e-05):
    m = jnp.mean(x, axis=axis, keepdims=True)
    v = jnp.var(x, axis=axis, keepdims=True)
    return (x - m) / jnp.sqrt(v + eps)

def _scatter_add(tgt, idx, src, axis=0):
    return tgt.at[idx].add(src)

def _segment_sum(src, seg, n):
    return jax.ops.segment_sum(src, seg, n)
kernel_name = 'mk_decoder_preln_d1_seqx_r4_e6a87b'

def setup_inputs(seed: int=0):
    np.random.seed(seed)
    _w = jnp.asarray

    def _rec_inputs():
        import jax
        import jax.numpy as jnp
        _rk = jax.random.key(seed)
        x = 0.0001212 + 1 * jax.random.normal(jax.random.fold_in(_rk, 1), (4, 512, 512), jnp.float32)
        _lenS = 512 - jax.random.randint(jax.random.fold_in(_rk, 7), (4,), 0, max(1, 512 // 4) + 1, jnp.int32)
        _lenS2 = 512 - jax.random.randint(jax.random.fold_in(_rk, 8), (4,), 0, max(1, 512 // 4) + 1, jnp.int32)
        _ctx_2048P = jax.random.normal(jax.random.fold_in(_rk, 11), (4, 16, 512), jnp.float32)
        _ctx_2048c = jax.random.dirichlet(jax.random.fold_in(_rk, 511), 0.3 * jnp.ones((16,), jnp.float32), (4, 512))
        _ctx_2048t = jnp.einsum('bsk,bkd->bsd', _ctx_2048c, _ctx_2048P)
        _ctx_2048t = _ctx_2048t * jax.lax.rsqrt(jnp.mean(jnp.square(_ctx_2048t)) + 1e-12) * 0.953939
        ctx_2048 = 0.000173663 + 1.0001 * (_ctx_2048t + 0.3 * jax.random.normal(jax.random.fold_in(_rk, 611), (4, 512, 512), jnp.float32))
        return (x, ctx_2048)
    x, ctx_2048 = _rec_inputs()

    def _L0_attn_setup():
        import jax, jax.numpy as jnp
        import numpy as np
        B, T, D = (4, 1024, 512)
        LAYER_ID, N_LAYERS = (0, 12)
        LN_EPS = 1e-05

        def _wkv(w, u, k, v):
            Bb, Tt, Dd = k.shape
            neg_ew = -jnp.exp(w)

            def step(carry, kv):
                aa, bb, pp = carry
                kt, vt = kv
                qt = jnp.maximum(pp, kt + u)
                e1 = jnp.exp(pp - qt)
                e2 = jnp.exp(kt + u - qt)
                out = (e1 * aa + e2 * vt) / (e1 * bb + e2)
                pp_new = jnp.maximum(pp + neg_ew, kt)
                f1 = jnp.exp(pp - pp_new)
                f2 = jnp.exp(kt - pp_new)
                return ((f1 * aa + f2 * vt, f1 * bb + f2, pp_new), out)
            init = (jnp.zeros((Bb, Dd), k.dtype), jnp.zeros((Bb, Dd), k.dtype), jnp.full((Bb, Dd), -1e+38, k.dtype))
            kT = jnp.swapaxes(k, 0, 1)
            vT = jnp.swapaxes(v, 0, 1)
            _, outT = jax.lax.scan(step, init, (kT, vT))
            return jnp.swapaxes(outT, 0, 1)
        key = jax.random.key(seed)
        ks = jax.random.split(key, 9)
        s = 0.02
        x = jax.random.normal(ks[0], (B, T, D), jnp.float32)
        Wk = jax.random.normal(ks[1], (D, D), jnp.float32) * s
        Wv = jax.random.normal(ks[2], (D, D), jnp.float32) * s
        Wr = jax.random.normal(ks[3], (D, D), jnp.float32) * s
        Wo = jax.random.normal(ks[4], (D, D), jnp.float32) * s
        tm_k = jax.random.uniform(ks[5], (1, 1, D), jnp.float32)
        tm_v = jax.random.uniform(ks[6], (1, 1, D), jnp.float32)
        tm_r = jax.random.uniform(ks[7], (1, 1, D), jnp.float32)
        ratio_0_to_1 = LAYER_ID / max(N_LAYERS - 1, 1)
        ratio_1_to_almost_0 = 1.0 - LAYER_ID / N_LAYERS
        i = jnp.arange(D, dtype=jnp.float32)
        time_decay = -5.0 + 8.0 * (i / (D - 1)) ** (0.7 + 1.3 * ratio_0_to_1)
        zigzag = (jnp.arange(D) % 3 - 1).astype(jnp.float32) * ratio_1_to_almost_0
        time_first = jnp.full((D,), jnp.log(jnp.float32(0.3))) + zigzag
        ln_g = jnp.ones((D,), jnp.float32)
        ln_b = jnp.zeros((D,), jnp.float32)
        return {'x': x, 'Wk': Wk, 'Wv': Wv, 'Wr': Wr, 'Wo': Wo, 'tm_k': tm_k, 'tm_v': tm_v, 'tm_r': tm_r, 'time_decay': time_decay, 'time_first': time_first, 'ln_g': ln_g, 'ln_b': ln_b}
    _L0_attn_all = _L0_attn_setup()
    _L0_attn_in = {k: v for k, v in _L0_attn_all.items() if k in ('Wk', 'Wv', 'Wr', 'Wo', 'tm_k', 'tm_v', 'tm_r', 'time_decay', 'time_first', 'ln_g', 'ln_b')}
    del _L0_attn_all

    def _L0_xattn_setup():
        import jax, jax.numpy as jnp
        import numpy as np
        B_DIM, T_DIM, C_DIM = (16, 256, 512)

        def _wkv(w, u, k, v):
            Bn, Tn, Cn = k.shape
            NEG_INF = jnp.float32(-1e+38)

            def step(carry, kv_t):
                p, q, o = carry
                kt, vt = kv_t
                no = jnp.maximum(o, u + kt)
                A = jnp.exp(o - no)
                E = jnp.exp(u + kt - no)
                y = (A * p + E * vt) / (A * q + E)
                no2 = jnp.maximum(w + o, kt)
                A2 = jnp.exp(w + o - no2)
                E2 = jnp.exp(kt - no2)
                return ((A2 * p + E2 * vt, A2 * q + E2, no2), y)
            init = (jnp.zeros((Bn, Cn), k.dtype), jnp.zeros((Bn, Cn), k.dtype), jnp.full((Bn, Cn), NEG_INF, k.dtype))
            kT = jnp.moveaxis(k, 1, 0)
            vT = jnp.moveaxis(v, 1, 0)
            _, yT = jax.lax.scan(step, init, (kT, vT))
            return jnp.moveaxis(yT, 0, 1)
        key = jax.random.key(seed)
        k1, k2, k3, k4 = jax.random.split(key, 4)
        w = -jnp.exp(jax.random.normal(k1, (C_DIM,), jnp.float32))
        u = jax.random.normal(k2, (C_DIM,), jnp.float32)
        k = jax.random.normal(k3, (B_DIM, T_DIM, C_DIM), jnp.float32)
        v = jax.random.normal(k4, (B_DIM, T_DIM, C_DIM), jnp.float32)
        return {'B': B_DIM, 'T': T_DIM, 'C': C_DIM, 'w': w, 'u': u, 'k': k, 'v': v}
    _L0_xattn_all = _L0_xattn_setup()
    _L0_xattn_in = {k: v for k, v in _L0_xattn_all.items() if k in ('w', 'u')}
    del _L0_xattn_all

    def _L0_ffn_setup():
        import jax, jax.numpy as jnp
        import numpy as np
        HIDDEN = 512
        INTER = 1408
        B, S = (2, 512)

        def _ternary(key, shape):
            return jax.random.randint(key, shape, -1, 2).astype(jnp.float32)
        key = jax.random.key(seed)
        ks = jax.random.split(key, 7)
        x = jax.random.normal(ks[0], (B, S, HIDDEN), dtype=jnp.float32)
        gate_w = _ternary(ks[1], (INTER, HIDDEN))
        up_w = _ternary(ks[2], (INTER, HIDDEN))
        down_w = _ternary(ks[3], (HIDDEN, INTER))
        gate_s = jax.random.uniform(ks[4], (INTER,), minval=0.01, maxval=0.1, dtype=jnp.float32)
        up_s = jax.random.uniform(ks[5], (INTER,), minval=0.01, maxval=0.1, dtype=jnp.float32)
        down_s = jax.random.uniform(ks[6], (HIDDEN,), minval=0.01, maxval=0.1, dtype=jnp.float32)
        return {'x': x, 'gate_w': gate_w, 'up_w': up_w, 'down_w': down_w, 'gate_s': gate_s, 'up_s': up_s, 'down_s': down_s}
    _L0_ffn_all = _L0_ffn_setup()
    _L0_ffn_in = {k: v for k, v in _L0_ffn_all.items() if k in ('gate_w', 'up_w', 'down_w', 'gate_s', 'up_s', 'down_s')}
    del _L0_ffn_all
    return {'x': x, 'ctx_2048': ctx_2048, 'L0_attn_Wk': _L0_attn_in['Wk'], 'L0_attn_Wv': _L0_attn_in['Wv'], 'L0_attn_Wr': _L0_attn_in['Wr'], 'L0_attn_Wo': _L0_attn_in['Wo'], 'L0_attn_tm_k': _L0_attn_in['tm_k'], 'L0_attn_tm_v': _L0_attn_in['tm_v'], 'L0_attn_tm_r': _L0_attn_in['tm_r'], 'L0_attn_time_decay': _L0_attn_in['time_decay'], 'L0_attn_time_first': _L0_attn_in['time_first'], 'L0_attn_ln_g': _L0_attn_in['ln_g'], 'L0_attn_ln_b': _L0_attn_in['ln_b'], 'L0_xattn_w': _L0_xattn_in['w'], 'L0_xattn_u': _L0_xattn_in['u'], 'L0_ffn_gate_w': _L0_ffn_in['gate_w'], 'L0_ffn_up_w': _L0_ffn_in['up_w'], 'L0_ffn_down_w': _L0_ffn_in['down_w'], 'L0_ffn_gate_s': _L0_ffn_in['gate_s'], 'L0_ffn_up_s': _L0_ffn_in['up_s'], 'L0_ffn_down_s': _L0_ffn_in['down_s']}

def reference(x, ctx_2048, L0_attn_Wk, L0_attn_Wv, L0_attn_Wr, L0_attn_Wo, L0_attn_tm_k, L0_attn_tm_v, L0_attn_tm_r, L0_attn_time_decay, L0_attn_time_first, L0_attn_ln_g, L0_attn_ln_b, L0_xattn_w, L0_xattn_u, L0_ffn_gate_w, L0_ffn_up_w, L0_ffn_down_w, L0_ffn_gate_s, L0_ffn_up_s, L0_ffn_down_s):
    import jax
    import jax.numpy as jnp

    def _L0_attn_ref(x, Wk, Wv, Wr, Wo, tm_k, tm_v, tm_r, time_decay, time_first, ln_g, ln_b):
        import jax, jax.numpy as jnp
        import numpy as np
        B, T, D = (4, 1024, 512)
        LAYER_ID, N_LAYERS = (0, 12)
        LN_EPS = 1e-05

        def _wkv(w, u, k, v):
            Bb, Tt, Dd = k.shape
            neg_ew = -jnp.exp(w)

            def step(carry, kv):
                aa, bb, pp = carry
                kt, vt = kv
                qt = jnp.maximum(pp, kt + u)
                e1 = jnp.exp(pp - qt)
                e2 = jnp.exp(kt + u - qt)
                out = (e1 * aa + e2 * vt) / (e1 * bb + e2)
                pp_new = jnp.maximum(pp + neg_ew, kt)
                f1 = jnp.exp(pp - pp_new)
                f2 = jnp.exp(kt - pp_new)
                return ((f1 * aa + f2 * vt, f1 * bb + f2, pp_new), out)
            init = (jnp.zeros((Bb, Dd), k.dtype), jnp.zeros((Bb, Dd), k.dtype), jnp.full((Bb, Dd), -1e+38, k.dtype))
            kT = jnp.swapaxes(k, 0, 1)
            vT = jnp.swapaxes(v, 0, 1)
            _, outT = jax.lax.scan(step, init, (kT, vT))
            return jnp.swapaxes(outT, 0, 1)
        xs = jnp.pad(x, ((0, 0), (1, 0), (0, 0)))[:, :-1, :]
        xk = x * tm_k + xs * (1.0 - tm_k)
        xv = x * tm_v + xs * (1.0 - tm_v)
        xr = x * tm_r + xs * (1.0 - tm_r)
        k = jnp.einsum('btd,ed->bte', xk, Wk)
        v = jnp.einsum('btd,ed->bte', xv, Wv)
        r = jax.nn.sigmoid(jnp.einsum('btd,ed->bte', xr, Wr))
        wkv = _wkv(time_decay, time_first, k, v)
        mu = jnp.mean(wkv, axis=-1, keepdims=True)
        var = jnp.mean(jnp.square(wkv - mu), axis=-1, keepdims=True)
        ln = (wkv - mu) * jax.lax.rsqrt(var + LN_EPS) * ln_g + ln_b
        rwkv = r * ln
        return jnp.einsum('btd,ed->bte', rwkv, Wo)

    def _L0_xattn_ref(B, T, C, w, u, k, v):
        import jax, jax.numpy as jnp
        import numpy as np
        B_DIM, T_DIM, C_DIM = (16, 256, 512)

        def _wkv(w, u, k, v):
            Bn, Tn, Cn = k.shape
            NEG_INF = jnp.float32(-1e+38)

            def step(carry, kv_t):
                p, q, o = carry
                kt, vt = kv_t
                no = jnp.maximum(o, u + kt)
                A = jnp.exp(o - no)
                E = jnp.exp(u + kt - no)
                y = (A * p + E * vt) / (A * q + E)
                no2 = jnp.maximum(w + o, kt)
                A2 = jnp.exp(w + o - no2)
                E2 = jnp.exp(kt - no2)
                return ((A2 * p + E2 * vt, A2 * q + E2, no2), y)
            init = (jnp.zeros((Bn, Cn), k.dtype), jnp.zeros((Bn, Cn), k.dtype), jnp.full((Bn, Cn), NEG_INF, k.dtype))
            kT = jnp.moveaxis(k, 1, 0)
            vT = jnp.moveaxis(v, 1, 0)
            _, yT = jax.lax.scan(step, init, (kT, vT))
            return jnp.moveaxis(yT, 0, 1)
        return _wkv(w, u, k, v)

    def _L0_ffn_ref(x, gate_w, up_w, down_w, gate_s, up_s, down_s):
        import jax, jax.numpy as jnp
        import numpy as np
        HIDDEN = 512
        INTER = 1408
        B, S = (2, 512)

        def _ternary(key, shape):
            return jax.random.randint(key, shape, -1, 2).astype(jnp.float32)
        b, s, h = x.shape
        xf = x.reshape(b * s, h)
        g = jnp.einsum('th,ih->ti', xf, gate_w) * gate_s
        u = jnp.einsum('th,ih->ti', xf, up_w) * up_s
        hdn = jax.nn.silu(g) * u
        out = jnp.einsum('ti,hi->th', hdn, down_w) * down_s
        return out.reshape(b, s, -1)
    x = x + _L0_attn_ref(_layernorm(x, axis=-1), L0_attn_Wk, L0_attn_Wv, L0_attn_Wr, L0_attn_Wo, L0_attn_tm_k, L0_attn_tm_v, L0_attn_tm_r, L0_attn_time_decay, L0_attn_time_first, L0_attn_ln_g, L0_attn_ln_b)
    x = x + _L0_xattn_ref(4, 512, 512, L0_xattn_w, L0_xattn_u, _layernorm(x, axis=-1), ctx_2048)
    x = x + _L0_ffn_ref(_layernorm(x, axis=-1), L0_ffn_gate_w, L0_ffn_up_w, L0_ffn_down_w, L0_ffn_gate_s, L0_ffn_up_s, L0_ffn_down_s)
    return x

_drawn_inputs = setup_inputs


def setup_inputs(seed=0):
    import zlib

    import numpy as np

    out = dict(_drawn_inputs(seed))
    spreads = {'L0_attn_ln_g': (1.0, 0.2), 'L0_attn_ln_b': (0.0, 0.364)}
    factors = {'L0_attn_time_decay': 200.0, 'L0_attn_time_first': 200.0}
    for name, (base, spread) in spreads.items():
        noise = np.random.default_rng([zlib.crc32(name.encode()), seed]).standard_normal(out[name].shape)
        drawn = base * np.exp(spread * noise) if base else spread * noise
        out[name] = jnp.asarray(drawn.astype(out[name].dtype))
    for name, factor in factors.items():
        out[name] = (out[name] * factor).astype(out[name].dtype)
    return out
```

```python
from contextlib import ExitStack

import concourse.bass as bass
from concourse import mybir

F32 = mybir.dt.float32
ALU = mybir.AluOpType
ACT = mybir.ActivationFunctionType

P = 128
EPS = 1e-5
LN2 = 0.6931471805599453
DEN_SHIFT = 31
EXP_SET = "natural_log_exp_and_others"
SILU_SET = "silu_and_others"

TM_K, TM_V, TM_R, DECAY, FIRST, LN_G, LN_B, XW, XU = range(9)
N_VEC = 9


def decoder_layer(nc, x, ctx_t, wk_t, wv_t, wr_t, wo_t, vecs_in, gate_t, up_t, down_t, ffn_scales, down_s, out):
    B, T, D = x.shape
    I = gate_t.shape[1]
    C = D // P
    TB = T // P
    NI = I // P
    HALF = T // 2
    HB = HALF // P
    NU = 2 * NI
    NB = 4

    USE_LN1, USE_R, USE_KV = 0, C, 2 * C
    USE_LN2, USE_BACK = 4 * C, 4 * C + TB
    USE_WO = USE_BACK + C
    USE_LN3 = USE_WO + TB
    USE_Y = USE_LN3 + C
    USE_LN4 = USE_Y + TB
    USES = USE_LN4 + C
    assert C == TB == NB and USES % NB == 0

    ctx = ExitStack()
    with ctx:
        def sb(name, *shape, dt=F32):
            return ctx.enter_context(nc.sbuf_tensor("t_" + name, [P, *shape], dt))

        wk, wv, wr, wo = (sb(n, C, D) for n in ("wk", "wv", "wr", "wo"))
        gate, up = sb("gate", C, I), sb("up", C, I)
        down = sb("down", NI, D)
        vecs = sb("vecs", N_VEC, C)
        fsc = sb("fsc", 2, NI)
        dsb = sb("dsb", D)
        ident = sb("ident", P)
        ramp = sb("ramp", T)
        mhalf = sb("mhalf", TB)
        den_bias = sb("den_bias", 1)
        ew, nw = sb("ew", C), sb("nw", C)
        half_g, half_b = sb("half_g", C), sb("half_b", C)
        neg_wp, bonus = sb("neg_wp", C), sb("bonus", C)
        keep, s_old, c_new = sb("keep", C), sb("s_old", C), sb("c_new", C)
        xres = sb("xres", TB, D)
        xf = sb("xf", TB, D)
        z = sb("z", TB, D)
        zt = sb("zt", C, T + 1)
        mixk = sb("mixk", C, T)
        mixv = sb("mixv", C, T)
        tanh_r = sb("tanh_r", C, T)
        z4 = sb("z4", C, T)
        slot = sb("slot", 2, 4, T)
        pmax = sb("pmax", T + 1)
        gap = sb("gap", T)
        inp = sb("inp", T)
        num_st, den_st = sb("num_st", T + 1), sb("den_st", T + 1)
        silu, h = sb("silu", 2, HALF), sb("h", 2, HALF)
        otile = sb("otile", 2, D)
        stats = sb("stats", TB, 6)
        mv = sb("mv", TB, 2)
        veps, rstd, nmr = sb("veps", TB), sb("rstd", TB), sb("nmr", TB)
        scrap = sb("scrap", 2)
        ctxt = mixv
        wkv = zt

        bank = [ctx.enter_context(nc.psum_tensor(f"bank{j}", [P, T], F32)) for j in range(NB)]
        gu = [ctx.enter_context(nc.psum_tensor(f"gu{j}", [P, 2, HALF], F32)) for j in range(2)]
        dacc = [ctx.enter_context(nc.psum_tensor(f"dacc{j}", [P, D], F32)) for j in range(HB)]

        per, head = {}, {}

        def sem(name, count, before=0):
            s = ctx.enter_context(nc.semaphore(name))
            per[s.name], head[s.name] = count, before
            return s

        x_in, ctx_in = sem("x_in", 16), sem("ctx_in", 16)
        filled = sem("filled", USES)
        stat_done, aggr_done = sem("stat_done", 4 * TB), sem("aggr_done", 4 * TB)
        veps_done, rstd_done = sem("veps_done", 4), sem("rstd_done", 4)
        nmr_done = sem("nmr_done", 1)
        z_done = sem("z_done", 3 * TB)
        zn_done = sem("zn_done", TB)
        zt_done = sem("zt_done", C)
        diff_done = sem("diff_done", C)
        mix_done = sem("mix_done", 3 * C)
        tanh_done = sem("tanh_done", C)
        pmax_done, gap_done = sem("pmax_done", C), sem("gap_done", C)
        newv_done = sem("newv_done", C)
        arg_done, exp_done = sem("arg_done", 4 * C), sem("exp_done", 4 * C)
        ks_done, xexp_done = sem("ks_done", C), sem("xexp_done", 2 * C)
        one_done = sem("one_done", C)
        inp_done = sem("inp_done", 2 * C)
        scan_done = sem("scan_done", 4 * C)
        part_done = sem("part_done", 3 * C)
        num_done, den_done = sem("num_done", 2 * C), sem("den_done", 2 * C)
        log_done, rec_done = sem("log_done", 2 * C), sem("rec_done", 2 * C)
        refine_done = sem("refine_done", 4 * C)
        wkv_done = sem("wkv_done", 2 * C)
        lnt_done, rw_done = sem("lnt_done", C), sem("rw_done", C)
        x1_done, xf_done = sem("x1_done", TB), sem("xf_done", TB)
        z4_done = sem("z4_done", C)
        gu_filled = [sem(f"gu_filled{j}", NU // 2) for j in range(2)]
        silu_done, h_done, downed = sem("silu_done", NU), sem("h_done", NU), sem("downed", NU)
        oscaled = sem("oscaled", TB)
        o_done = sem("o_done", TB)
        stored = [sem(f"stored{j}", 16 * TB // 2, 16) for j in range(2)]
        vec_in = sem("vec_in", 0)
        w_in = {n: sem(f"{n}_in", 0) for n in ("wr", "wk", "wv", "wo", "gate", "up", "down")}
        ident_done, const_done, pre_act, pre_dve = (
            sem("ident_done", 0), sem("const_done", 0), sem("pre_act", 0), sem("pre_dve", 0))

        def need(eng, s, b, k):
            v = b * per[s.name] + k + head[s.name]
            if isinstance(v, int) and v <= 0:
                return
            eng.wait_ge(s, v)

        def need_filled(eng, b, n):
            need(eng, filled, b, n + 1)

        READ = [(zt_done, c) for c in range(C)] + [(tanh_done, c) for c in range(C)]
        for c in range(C):
            READ += [(gap_done, c), (newv_done, c)]
        READ += [(s, c) for s in (zn_done, lnt_done, x1_done, ks_done, xf_done, z4_done) for c in range(C)]
        assert len(READ) == USES

        def need_drained(eng, b, n):
            s, c = READ[n - NB]
            need(eng, s, b if n >= NB else b - 1, c + 1)

        A_STEPS = ["ln1", "mix", "r"]
        A_STEPS += ["front0"]
        for c in range(C):
            A_STEPS += [f"front{c + 1}"] * (c + 1 < C) + [f"back{c}", f"fin{c}"]
        A_STEPS += ["ln2", "wo", "ln3", "xfront0"]
        for c in range(C):
            A_STEPS += [f"xfront{c + 1}"] * (c + 1 < C) + [f"xback{c}", f"xfin{c}"]
        A_STEPS += ["y", "ln4"]
        AHEAD = {"mix": 1, "front1": 1, "fin0": 2, "fin1": 2, "fin2": 2, "fin3": 2, "wo": 1, "ln3": 1,
                 "xfront0": 1, "xfin0": 2, "xfin1": 2, "xfin2": 2, "xfin3": 2, "y": 1}
        assert sum(AHEAD.values()) == NU, sum(AHEAD.values())
        F_STEPS = []
        for u in range(NU):
            F_STEPS += [f"unit{u}"]
            if u % NI == 0 and u:
                F_STEPS += [f"out{u // NI - 1}"]
        F_STEPS += ["last", "out1"]

        def overlapped():
            steps, f = [], 0
            left = list(F_STEPS)
            for s in A_STEPS:
                for _ in range(AHEAD.get(s, 0)):
                    steps.append(left.pop(0))
                    while left and not left[0].startswith("unit"):
                        steps.append(left.pop(0))
                steps.append(s)
            assert not left
            return steps

        ORDER_AF = overlapped()

        def run(eng, step):
            for s in A_STEPS:
                step(s, 0, None)
            with eng.Fori(1, B) as b:
                for s in ORDER_AF:
                    step(s, b, b - 1)
            for s in F_STEPS:
                step(s, None, B - 1)

        block = ctx.enter_context(nc.Block())

        @block.sync
        def _(sp):
            sp.dma_start(vecs[:, :, :], vecs_in.rearrange("p (n c) -> p n c", c=C)).then_inc(vec_in, 16)

            def load_x(b):
                need(sp, xf_done, b, 0)
                src = x[b, :, :] if isinstance(b, int) else x[bass.ds(b, 1), :, :].rearrange("a t d -> (a t) d")
                sp.dma_start(xres[:, :, :], src.rearrange("(n p) d -> p n d", p=P)).then_inc(x_in, 16)

            def load_ctx(b):
                need_filled(sp, b, USE_KV + 2 * C - 1)
                src = ctx_t[b, :, :] if isinstance(b, int) else ctx_t[bass.ds(b, 1), :, :].rearrange("a d t -> (a d) t")
                sp.dma_start(ctxt[:, :, :], src.rearrange("(c p) t -> p c t", p=P)).then_inc(ctx_in, 16)

            load_x(0)
            for name, tile, src in (("wr", wr, wr_t), ("wk", wk, wk_t), ("wv", wv, wv_t), ("wo", wo, wo_t)):
                sp.dma_start(tile[:, :, :], src.rearrange("(c p) e -> p c e", p=P)).then_inc(w_in[name], 16)
            sp.dma_start(fsc[:, :, :], ffn_scales.rearrange("p (n i) -> p n i", i=NI)).then_inc(stored[0], 16)
            sp.dma_start(dsb[:, :], down_s.to_broadcast([P, D])).then_inc(stored[1], 16)
            for name, tile, src in (("gate", gate, gate_t), ("up", up, up_t)):
                sp.dma_start(tile[:, :, :], src.rearrange("(c p) i -> p c i", p=P)).then_inc(w_in[name], 16)
            sp.dma_start(down[:, :, :], down_t.rearrange("(i p) e -> p i e", p=P)).then_inc(w_in["down"], 16)

            def step(s, b, f):
                if s == "ln1" and not (isinstance(b, int) and b == 0):
                    load_x(b)
                if s == "back3":
                    load_ctx(b)
                if s.startswith("out"):
                    for j in range(HB):
                        n = int(s[3:]) * HB + j
                        need(sp, o_done, f, n + 1)
                        dst = out[f, :, :] if isinstance(f, int) else out[bass.ds(f, 1), :, :].rearrange("a t d -> (a t) d")
                        sp.dma_start(dst[n * P:(n + 1) * P, :], otile[:, n % 2, :]).then_inc(stored[n % 2], 16)

            run(sp, step)
            for j in range(2):
                need(sp, stored[j], B, 0)

        @block.gpsimd
        def _(pool):
            pool.memset(ident[:, :], 0.0).then_inc(ident_done, 1)
            pool.wait_ge(ident_done, 1)
            pool.affine_select(out=ident[:, :], in_=ident[:, :], compare_op=ALU.not_equal, fill=1.0,
                               base=0, pattern=[[-1, P]], channel_multiplier=1).then_inc(ident_done, 1)
            pool.memset(mhalf[:, :], -0.5).then_inc(ident_done, 1)
            pool.wait_ge(ident_done, 3)

            def step(s, b, f):
                if s in ("ln1", "ln2", "ln3", "ln4"):
                    k = int(s[2:])
                    need(pool, veps_done, b, k)
                    pool.tensor_tensor(rstd[:, :], veps[:, :], mhalf[:, :], ALU.pow).then_inc(rstd_done, 1)

            run(pool, step)

        @block.tensor
        def _(pe):
            pe.wait_ge(ident_done, 2)

            def turn(b, use, tiles):
                for m in range(NB):
                    need_drained(pe, b, use + m)
                    for k in range(NB):
                        last = pe.transpose(bank[m][:, k * P:(k + 1) * P], tiles(m, k), ident[:, :])
                    last.then_inc(filled, 1)

            def project(b, n, w, c, src):
                need_drained(pe, b, n)
                for k in range(C):
                    last = pe.matmul(bank[n % NB][:, :], w[:, k, c * P:(c + 1) * P], src[:, k, :],
                                     start=(k == 0), stop=(k == C - 1))
                last.then_inc(filled, 1)

            def down_unit(u, f):
                hf, i = divmod(u, NI)
                need(pe, h_done, f, u + 1)
                if i == 0 and hf:
                    need(pe, oscaled, f, hf * HB)
                for j in range(HB):
                    last = pe.matmul(dacc[j][:, :], h[:, u % 2, j * P:(j + 1) * P], down[:, i, :],
                                     start=(i == 0), stop=(i == NI - 1))
                last.then_inc(downed, 1)

            def step(s, b, f):
                first = isinstance(b, int) and b == 0
                if s == "ln1":
                    need(pe, z_done, b, TB)
                    turn(b, USE_LN1, lambda m, k: z[:, k, m * P:(m + 1) * P])
                elif s == "r":
                    if first:
                        pe.wait_ge(w_in["wr"], 16)
                    need(pe, mix_done, b, 3 * C)
                    for c in range(C):
                        project(b, USE_R + c, wr, c, z)
                elif s.startswith("front"):
                    c = int(s[5:])
                    if first and c == 0:
                        pe.wait_ge(w_in["wk"], 16)
                    project(b, USE_KV + 2 * c, wk, c, mixk)
                    if first and c == 0:
                        pe.wait_ge(w_in["wv"], 16)
                    project(b, USE_KV + 2 * c + 1, wv, c, mixv)
                elif s == "ln2":
                    need(pe, wkv_done, b, C)
                    turn(b, USE_LN2, lambda m, k: wkv[:, k, 1 + m * P:1 + (m + 1) * P])
                    need(pe, zn_done, b, TB)
                    turn(b, USE_BACK, lambda m, k: z[:, k, m * P:(m + 1) * P])
                elif s == "wo":
                    if first:
                        pe.wait_ge(w_in["wo"], 16)
                    need(pe, rw_done, b, C)
                    for m in range(TB):
                        need_drained(pe, b, USE_WO + m)
                        for k in range(C):
                            last = pe.matmul(bank[m][:, :], mixk[:, k, m * P:(m + 1) * P], wo[:, k, :],
                                             start=(k == 0), stop=(k == C - 1))
                        last.then_inc(filled, 1)
                elif s == "ln3":
                    need(pe, z_done, b, 2 * TB)
                    turn(b, USE_LN3, lambda m, k: z[:, k, m * P:(m + 1) * P])
                elif s == "y":
                    need(pe, wkv_done, b, 2 * C)
                    turn(b, USE_Y, lambda m, k: wkv[:, k, 1 + m * P:1 + (m + 1) * P])
                elif s == "ln4":
                    need(pe, z_done, b, 3 * TB)
                    turn(b, USE_LN4, lambda m, k: z[:, k, m * P:(m + 1) * P])
                elif s.startswith("unit"):
                    u = int(s[4:])
                    hf, i = divmod(u, NI)
                    if u == 0:
                        need(pe, z4_done, f, C)
                        pe.wait_ge(w_in["gate"], 16)
                        pe.wait_ge(w_in["up"], 16)
                        pe.wait_ge(w_in["down"], 16)
                    if u >= 2:
                        need(pe, h_done, f, u - 1)
                    for side, w in enumerate((gate, up)):
                        for k in range(C):
                            last = pe.matmul(gu[u % 2][:, side, :], w[:, k, i * P:(i + 1) * P],
                                             z4[:, k, hf * HALF:(hf + 1) * HALF], start=(k == 0), stop=(k == C - 1))
                    last.then_inc(gu_filled[u % 2], 1)
                    if u:
                        down_unit(u - 1, f)
                elif s == "last":
                    down_unit(NU - 1, f)

            run(pe, step)

        @block.scalar
        def _(act):
            loaded = []

            def table(name):
                if loaded[-1:] != [name]:
                    act.preload_act_table_set(name)
                    loaded.append(name)

            table(EXP_SET)
            act.wait_ge(vec_in, 16)
            act.wait_ge(pre_dve, 1)
            act.activation(ew[:, :], ew[:, :], ACT.Exp).then_inc(pre_act, 1)
            act.activation(keep[:, :], keep[:, :], ACT.Exp).then_inc(pre_act, 1)
            act.activation(s_old[:, :], s_old[:, :], ACT.Exp, scale=-1.0).then_inc(pre_act, 1)
            act.wait_ge(stored[0], 16)

            def step(s, b, f):
                if s == "ln1":
                    table(EXP_SET)
                    for c in range(C):
                        need_filled(act, b, USE_LN1 + c)
                        act.activation(zt[:, c, 1:], bank[c][:, :], ACT.Copy).then_inc(zt_done, 1)
                elif s == "r":
                    table(SILU_SET)
                    for c in range(C):
                        need_filled(act, b, USE_R + c)
                        act.activation(tanh_r[:, c, :], bank[c][:, :], ACT.Tanh, scale=0.5).then_inc(tanh_done, 1)
                elif s.startswith("front"):
                    c = int(s[5:])
                    table(EXP_SET)
                    for m, sign in enumerate((-1.0, 1.0, 1.0, -1.0)):
                        need(act, arg_done, b, 4 * c + m + 1)
                        act.activation(slot[:, c % 2, m, :], slot[:, c % 2, m, :], ACT.Exp, scale=sign).then_inc(exp_done, 1)
                elif s.startswith("back"):
                    c = int(s[4:])
                    table(EXP_SET)
                    need(act, den_done, b, c + 1)
                    act.activation(slot[:, c % 2, 1, :], slot[:, c % 2, 0, :], ACT.Ln, scale=2.0 ** -DEN_SHIFT).then_inc(log_done, 1)
                    need(act, log_done, b, c + 1)
                    act.activation(slot[:, c % 2, 1, :], slot[:, c % 2, 1, :], ACT.Exp, scale=-1.0,
                                   bias=den_bias[:, :]).then_inc(rec_done, 1)
                elif s == "ln2":
                    need(act, nmr_done, b, 1)
                    for t in range(TB):
                        need_filled(act, b, USE_LN2 + t)
                        act.activation(z[:, t, :], bank[t][:, :], ACT.Identity, scale=rstd[:, t:t + 1],
                                       bias=nmr[:, t:t + 1]).then_inc(zn_done, 1)
                    for c in range(C):
                        need_filled(act, b, USE_BACK + c)
                        act.activation(mixk[:, c, :], bank[c][:, :], ACT.Identity, scale=half_g[:, c:c + 1],
                                       bias=half_b[:, c:c + 1]).then_inc(lnt_done, 1)
                elif s.startswith("xfront"):
                    c = int(s[6:])
                    table(EXP_SET)
                    need(act, ks_done, b, c + 1)
                    act.activation(slot[:, c % 2, 1, 1:], slot[:, c % 2, 0, 1:], ACT.Exp, bias=c_new[:, c:c + 1]).then_inc(xexp_done, 1)
                    act.activation(slot[:, c % 2, 3, :], slot[:, c % 2, 0, :], ACT.Exp).then_inc(xexp_done, 1)
                elif s.startswith("xback"):
                    c = int(s[5:])
                    table(EXP_SET)
                    need(act, den_done, b, C + c + 1)
                    act.activation(slot[:, c % 2, 1, :], slot[:, c % 2, 3, :], ACT.Ln).then_inc(log_done, 1)
                    need(act, log_done, b, C + c + 1)
                    act.activation(slot[:, c % 2, 1, :], slot[:, c % 2, 1, :], ACT.Exp, scale=-1.0).then_inc(rec_done, 1)
                elif s == "ln4":
                    table(EXP_SET)
                    for c in range(C):
                        need_filled(act, b, USE_LN4 + c)
                        act.activation(z4[:, c, :], bank[c][:, :], ACT.Copy).then_inc(z4_done, 1)
                elif s.startswith("unit"):
                    u = int(s[4:])
                    table(SILU_SET)
                    need(act, gu_filled[u % 2], f, u // 2 + 1)
                    act.activation(silu[:, u % 2, :], gu[u % 2][:, 0, :], ACT.Silu,
                                   scale=fsc[:, 0, u % NI:u % NI + 1]).then_inc(silu_done, 1)

            run(act, step)

        @block.vector
        def _(dve):
            dve.memset(zt[:, :, 0:1], 0.0)
            dve.memset(pmax[:, 0:1], -1e38)
            dve.memset(num_st[:, 0:1], 0.0)
            dve.memset(den_st[:, 0:1], 0.0)
            dve.memset(scrap[:, :], 0.0)
            dve.memset(gap[:, :], 1.0)
            dve.memset(den_bias[:, :], -DEN_SHIFT * LN2).then_inc(const_done, 1)
            dve.wait_ge(const_done, 1)
            dve.tensor_tensor_scan(ramp[:, :], gap[:, :], gap[:, :], -1.0, ALU.add, ALU.mult).then_inc(const_done, 1)
            dve.wait_ge(vec_in, 16)
            dve.tensor_scalar(neg_wp[:, :], vecs[:, XW, :], 0.0, -1.0, ALU.max, ALU.mult).then_inc(const_done, 1)
            dve.tensor_scalar(keep[:, :], vecs[:, XW, :], 0.0, None, ALU.min).then_inc(const_done, 1)
            dve.wait_ge(const_done, 4)
            dve.tensor_tensor(bonus[:, :], vecs[:, XU, :], neg_wp[:, :], ALU.subtract).then_inc(const_done, 1)
            dve.wait_ge(const_done, 5)
            dve.tensor_scalar(ew[:, :], vecs[:, DECAY, :], 88.0, None, ALU.min)
            dve.tensor_scalar(c_new[:, :], bonus[:, :], 0.0, None, ALU.min)
            dve.tensor_scalar(half_g[:, :], vecs[:, LN_G, :], 0.5, None, ALU.mult)
            dve.tensor_scalar(half_b[:, :], vecs[:, LN_B, :], 0.5, None, ALU.mult)
            dve.tensor_scalar(s_old[:, :], bonus[:, :], 0.0, None, ALU.max).then_inc(pre_dve, 1)
            dve.wait_ge(pre_act, 3)
            dve.tensor_scalar(nw[:, :], ew[:, :], -1.0, None, ALU.mult).then_inc(const_done, 1)
            dve.wait_ge(const_done, 6)
            dve.wait_ge(stored[0], 16)
            dve.wait_ge(stored[1], 16)

            def normalise_stats(b, k, tile, ready):
                for t in range(TB):
                    ready(t)
                    dve.bn_stats(stats[:, t, :], tile(t)).then_inc(stat_done, 1)
                need(dve, stat_done, b, (k + 1) * TB)
                dve.memset(scrap[:, 0:1], 0.0)
                for t in range(TB):
                    dve.bn_aggr(mv[:, t, :], stats[:, t, :]).then_inc(aggr_done, 1)
                need(dve, aggr_done, b, (k + 1) * TB)
                dve.tensor_scalar(veps[:, :], mv[:, :, 1], EPS, None, ALU.add).then_inc(veps_done, 1)
                need(dve, rstd_done, b, k + 1)

            def normalise(b, k, src):
                for t in range(TB):
                    dve.tensor_scalar(z[:, t, :], src[:, t, :], mv[:, t, 0:1], rstd[:, t:t + 1],
                                      ALU.subtract, ALU.mult).then_inc(z_done, 1)

            def refine(b, c, r, num, den):
                sl = slot[:, c % 2]
                need(dve, rec_done, b, r + 1)
                dve.tensor_tensor(sl[:, den, :], sl[:, den, :], sl[:, 1, :], ALU.mult).then_inc(refine_done, 1)
                dve.tensor_tensor(sl[:, num, :], sl[:, num, :], sl[:, 1, :], ALU.mult).then_inc(refine_done, 1)
                need(dve, refine_done, b, 2 * r + 2)
                dve.scalar_tensor_tensor(out=wkv[:, c, 1:], in0=sl[:, den, :], scalar=2.0, in1=sl[:, num, :],
                                         op0=ALU.subtract, op1=ALU.mult, reverse0=True).then_inc(wkv_done, 1)

            def step(s, b, f):
                if s == "ln1":
                    need(dve, x_in, b, 16)
                    normalise_stats(b, 0, lambda t: xres[:, t, :], lambda t: None)
                    need_filled(dve, b - 1, USE_LN4 + C - 1)
                    normalise(b, 0, xres)
                elif s == "mix":
                    need(dve, zt_done, b, C)
                    for c in range(C):
                        step_up = slot[:, c % 2, 0, :]
                        if c >= 2:
                            need(dve, mix_done, b, 3 * (c - 1))
                        dve.tensor_tensor(step_up, zt[:, c, 1:], zt[:, c, 0:T], ALU.subtract).then_inc(diff_done, 1)
                        need(dve, diff_done, b, c + 1)
                        for tm, dst in ((TM_R, z), (TM_K, mixk), (TM_V, mixv)):
                            dve.scalar_tensor_tensor(out=dst[:, c, :], in0=step_up, scalar=vecs[:, tm, c:c + 1],
                                                     in1=zt[:, c, 0:T], op0=ALU.mult, op1=ALU.add).then_inc(mix_done, 1)
                elif s.startswith("front"):
                    c = int(s[5:])
                    sl = slot[:, c % 2]
                    kb, k = bank[(USE_KV + 2 * c) % NB], USE_KV + 2 * c
                    need_filled(dve, b, k)
                    dve.tensor_tensor_scan(pmax[:, 1:], nw[:, c:c + 1].to_broadcast([P, T]), kb[:, :], -1e38,
                                           ALU.add, ALU.max).then_inc(pmax_done, 1)
                    need(dve, pmax_done, b, c + 1)
                    dve.tensor_tensor(gap[:, :], pmax[:, 0:T], kb[:, :], ALU.subtract).then_inc(gap_done, 1)
                    need(dve, gap_done, b, c + 1)
                    first = vecs[:, FIRST, c:c + 1]
                    dve.tensor_scalar(sl[:, 0, :], gap[:, :], nw[:, c:c + 1], 0.0, ALU.add, ALU.max).then_inc(arg_done, 1)
                    dve.tensor_scalar(sl[:, 1, :], gap[:, :], ew[:, c:c + 1], None, ALU.min).then_inc(arg_done, 1)
                    dve.tensor_scalar(sl[:, 2, :], gap[:, :], first, 0.0, ALU.subtract, ALU.min).then_inc(arg_done, 1)
                    dve.tensor_scalar(sl[:, 3, :], gap[:, :], first, 0.0, ALU.subtract, ALU.max).then_inc(arg_done, 1)
                elif s.startswith("back"):
                    c = int(s[4:])
                    sl = slot[:, c % 2]
                    n = USE_KV + 2 * c + 1
                    vb = bank[n % NB]
                    need_filled(dve, b, n)
                    need(dve, exp_done, b, 4 * c + 1)
                    dve.tensor_tensor(inp[:, :], sl[:, 0, :], vb[:, :], ALU.mult).then_inc(inp_done, 1)
                    need(dve, exp_done, b, 4 * c + 2)
                    dve.tensor_tensor_scan(den_st[:, 1:], sl[:, 1, :], sl[:, 0, :], 0.0, ALU.mult, ALU.add).then_inc(scan_done, 1)
                    need(dve, inp_done, b, c + 1)
                    dve.tensor_tensor_scan(num_st[:, 1:], sl[:, 1, :], inp[:, :], 0.0, ALU.mult, ALU.add).then_inc(scan_done, 1)
                    need(dve, exp_done, b, 4 * c + 4)
                    dve.tensor_tensor(gap[:, :], sl[:, 3, :], vb[:, :], ALU.mult).then_inc(newv_done, 1)
                    need(dve, scan_done, b, 2 * c + 2)
                    dve.tensor_tensor(sl[:, 0, :], sl[:, 2, :], den_st[:, 0:T], ALU.mult).then_inc(part_done, 1)
                    dve.tensor_tensor(sl[:, 2, :], sl[:, 2, :], num_st[:, 0:T], ALU.mult).then_inc(part_done, 1)
                    need(dve, part_done, b, 2 * c + 1)
                    dve.tensor_tensor(sl[:, 0, :], sl[:, 0, :], sl[:, 3, :], ALU.add).then_inc(den_done, 1)
                    need(dve, part_done, b, 2 * c + 2)
                    need(dve, newv_done, b, c + 1)
                    dve.tensor_tensor(sl[:, 2, :], sl[:, 2, :], gap[:, :], ALU.add).then_inc(num_done, 1)
                elif s.startswith("fin"):
                    c = int(s[3:])
                    need(dve, num_done, b, c + 1)
                    refine(b, c, c, 2, 0)
                elif s == "ln2":
                    normalise_stats(b, 1, lambda t: bank[t][:, :], lambda t: need_filled(dve, b, USE_LN2 + t))
                    dve.scalar_tensor_tensor(out=nmr[:, :], in0=mv[:, :, 0], scalar=-1.0, in1=rstd[:, :],
                                             op0=ALU.mult, op1=ALU.mult).then_inc(nmr_done, 1)
                    for c in range(C):
                        need(dve, lnt_done, b, c + 1)
                        dve.scalar_tensor_tensor(out=mixk[:, c, :], in0=tanh_r[:, c, :], scalar=1.0, in1=mixk[:, c, :],
                                                 op0=ALU.add, op1=ALU.mult).then_inc(rw_done, 1)
                elif s == "wo":
                    for t in range(TB):
                        need_filled(dve, b, USE_WO + t)
                        dve.tensor_tensor(xres[:, t, :], bank[t][:, :], xres[:, t, :], ALU.add).then_inc(x1_done, 1)
                elif s == "ln3":
                    normalise_stats(b, 2, lambda t: xres[:, t, :], lambda t: need(dve, x1_done, b, t + 1))
                    normalise(b, 2, xres)
                elif s.startswith("xfront"):
                    c = int(s[6:])
                    n = USE_LN3 + c
                    need_filled(dve, b, n)
                    dve.memset(slot[:, c % 2, 1, 0:1], 1.0).then_inc(one_done, 1)
                    dve.scalar_tensor_tensor(out=slot[:, c % 2, 0, :], in0=ramp[:, :], scalar=neg_wp[:, c:c + 1],
                                             in1=bank[n % NB][:, :], op0=ALU.mult, op1=ALU.add).then_inc(ks_done, 1)
                elif s.startswith("xback"):
                    c = int(s[5:])
                    sl = slot[:, c % 2]
                    if c == 0:
                        need(dve, ctx_in, b, 16)
                    v = ctxt[:, c, :]
                    decay = keep[:, c:c + 1].to_broadcast([P, T])
                    need(dve, xexp_done, b, 2 * c + 2)
                    dve.tensor_tensor(inp[:, :], sl[:, 3, :], v, ALU.mult).then_inc(inp_done, 1)
                    dve.tensor_tensor_scan(den_st[:, 1:], decay, sl[:, 3, :], 0.0, ALU.mult, ALU.add).then_inc(scan_done, 1)
                    need(dve, inp_done, b, C + c + 1)
                    dve.tensor_tensor_scan(num_st[:, 1:], decay, inp[:, :], 0.0, ALU.mult, ALU.add).then_inc(scan_done, 1)
                    need(dve, one_done, b, c + 1)
                    dve.tensor_tensor(sl[:, 2, :], sl[:, 1, :], v, ALU.mult).then_inc(part_done, 1)
                    need(dve, scan_done, b, 2 * C + 2 * c + 2)
                    dve.scalar_tensor_tensor(out=sl[:, 3, :], in0=den_st[:, 0:T], scalar=s_old[:, c:c + 1],
                                             in1=sl[:, 1, :], op0=ALU.mult, op1=ALU.add).then_inc(den_done, 1)
                    need(dve, part_done, b, 2 * C + c + 1)
                    dve.scalar_tensor_tensor(out=sl[:, 2, :], in0=num_st[:, 0:T], scalar=s_old[:, c:c + 1],
                                             in1=sl[:, 2, :], op0=ALU.mult, op1=ALU.add).then_inc(num_done, 1)
                elif s.startswith("xfin"):
                    c = int(s[4:])
                    need(dve, num_done, b, C + c + 1)
                    refine(b, c, C + c, 2, 3)
                elif s == "y":
                    if f is not None:
                        need(dve, o_done, f, TB)
                    for t in range(TB):
                        need_filled(dve, b, USE_Y + t)
                        dve.tensor_tensor(xf[:, t, :], bank[t][:, :], xres[:, t, :], ALU.add).then_inc(xf_done, 1)
                elif s == "ln4":
                    normalise_stats(b, 3, lambda t: xf[:, t, :], lambda t: need(dve, xf_done, b, t + 1))
                    normalise(b, 3, xf)
                elif s.startswith("unit"):
                    u = int(s[4:])
                    need(dve, silu_done, f, u + 1)
                    if u >= 2:
                        need(dve, downed, f, u - 1)
                    dve.scalar_tensor_tensor(out=h[:, u % 2, :], in0=gu[u % 2][:, 1, :],
                                             scalar=fsc[:, 1, u % NI:u % NI + 1], in1=silu[:, u % 2, :],
                                             op0=ALU.mult, op1=ALU.mult).then_inc(h_done, 1)
                elif s.startswith("out"):
                    hf = int(s[3:])
                    need(dve, downed, f, (hf + 1) * NI)
                    for j in range(HB):
                        n = hf * HB + j
                        need(dve, stored[n % 2], f, 16 * (n // 2))
                        dve.tensor_tensor(otile[:, n % 2, :], dacc[j][:, :], dsb[:, :], ALU.mult).then_inc(oscaled, 1)
                        need(dve, oscaled, f, n + 1)
                        dve.tensor_tensor(otile[:, n % 2, :], otile[:, n % 2, :], xf[:, n, :], ALU.add).then_inc(o_done, 1)

            run(dve, step)


def kernel(**inputs):
    import numpy as _np
    import concourse.bacc as _bacc
    from concourse import mybir as _mybir
    from concourse.bass_utils import run_bass_kernel_spmd as _run

    def columns(v):
        return _np.asarray(v).reshape(-1, P).T

    def turned(w):
        return _np.ascontiguousarray(_np.asarray(w).T)

    arrays = {
        "x": _np.ascontiguousarray(inputs["x"]),
        "ctx_t": _np.ascontiguousarray(_np.asarray(inputs["ctx_2048"]).transpose(0, 2, 1)),
        "wk_t": turned(inputs["L0_attn_Wk"]),
        "wv_t": turned(inputs["L0_attn_Wv"]),
        "wr_t": turned(inputs["L0_attn_Wr"]),
        "wo_t": turned(inputs["L0_attn_Wo"]),
        "vecs": _np.ascontiguousarray(_np.concatenate([columns(inputs[n]) for n in (
            "L0_attn_tm_k", "L0_attn_tm_v", "L0_attn_tm_r", "L0_attn_time_decay", "L0_attn_time_first",
            "L0_attn_ln_g", "L0_attn_ln_b", "L0_xattn_w", "L0_xattn_u")], axis=1)),
        "gate_t": turned(inputs["L0_ffn_gate_w"]),
        "up_t": turned(inputs["L0_ffn_up_w"]),
        "down_t": turned(inputs["L0_ffn_down_w"]),
        "ffn_scales": _np.ascontiguousarray(_np.concatenate(
            [columns(inputs["L0_ffn_gate_s"]), columns(inputs["L0_ffn_up_s"])], axis=1)),
        "down_s": _np.ascontiguousarray(_np.asarray(inputs["L0_ffn_down_s"]).reshape(1, -1)),
    }
    nc = _bacc.Bacc("TRN2", target_bir_lowering=False, num_devices=1)
    args = [nc.dram_tensor("in_" + n, a.shape, _mybir.dt.from_np(a.dtype), kind="ExternalInput").ap() for n, a in arrays.items()]
    out = nc.dram_tensor("out", arrays["x"].shape, _mybir.dt.float32, kind="ExternalOutput").ap()
    decoder_layer(nc, *args, out)
    r = _run(nc, [{"in_" + n: a for n, a in arrays.items()}], core_ids=[0])
    return r.results[0]["out"]
```

```python
from contextlib import ExitStack

import concourse.bass as bass
from concourse import mybir

F32 = mybir.dt.float32
F32R = mybir.dt.float32r
F32R_LOST = (1 << 12) - 1
I32 = mybir.dt.int32
AXIS_X = mybir.AxisListType.X
ALU = mybir.AluOpType
ACT = mybir.ActivationFunctionType

P = 128
EPS = 1e-5
LN2 = 0.6931471805599453
DEN_SHIFT = 31
EXP_SET = "natural_log_exp_and_others"
SILU_SET = "silu_and_others"

TM_K, TM_V, TM_R, DECAY, FIRST, LN_G, LN_B, XW, XU = range(9)
N_VEC = 9


def decoder_layer(nc, x, ctx_t, wk_t, wv_t, wr_t, wo_t, vecs_in, gate_t, up_t, down_t, ffn_scales, down_s, out):
    B, T, D = x.shape
    I = gate_t.shape[1]
    C = D // P
    TB = T // P
    NI = I // P
    HALF = T // 2
    HB = HALF // P
    NU = 2 * NI
    NB = 4

    BODY = """
        prod0 up0 silu0 xf_2 prod1 xf_3 silu1 up1 up2 rest0 up3 rest1 high0 high1 prod2 down0 silu2
        silu3 stat4_1 turn4_1 high2 up4 stat1_0 z4_1 stat1 down1 prod3 turn1 high3 silu4 silu5 up5
        rest2 mix_k mix_v rest3 down2 kv0 prod4 kv1 kv2 front0 back0 mix_r up6 high4 part0 high5
        prod5 down3 up7 front1 back1 silu6 part1 fin0 front2 fin1 kv3 back2 silu7 prod6 part2 front3
        back3 r0 part3 r1 rest4 r2 up8 r3 fin2 fin3 down4 tanh0 turn2 silu8 down5 down6 tanh1 tanh2
        tanh3 rest5 prod7 prod8 high6 up9 high7 up10 rest6 stat2 high8 return2 rest7 rest8 rw silu9
        prod9 down7 down8 wo up11 down9 x1_0 high9 down10 silu10 high10 prod10 up12 silu11 rest9
        rest10 x1_1 x1_2 x1_3 stat3 turn3 prod11 silu12 out0 high11 xfront0 up13 prod12 silu13 up14
        up15 rest11 silu14 xback0 prod13 down11 xpart0 high12 prod14 down12 xfront1 xfin0 rest12
        rest13 high13 xfront2 xback1 down13 up16 up17 up18 down14 silu15 high14 xpart1 prod15 xback2
        silu16 silu17 up19 rest14 xfin1 prod16 xpart2 xfront3 high15 prod17 xfin2 high16 rest15
        silu18 silu19 xback3 prod18 xpart3 down15 rest16 up20 down16 high17 high18 high19 silu20
        silu21 prod19 xfin3 y rest17 high20 rest18 up21 xf_0 xf_1 rest19 prod20 down17 down18
        stat4_0 down19 prod21 rest20 high21 rest21 turn4_0 down20 z4_0 down21 out1
        """.split()
    FIRST_ORDER = """
        stat1_0 stat1 turn1 mix_k mix_v kv0 kv1 kv2 mix_r front0 back0 part0 kv3 front1 fin0 back1
        part1 r0 r1 front2 fin1 back2 part2 r2 front3 tanh0 r3 fin2 back3 part3 weigh0 tanh1 tanh2
        fin3 weigh3 turn2 tanh3 stat2 weigh6 weigh9 weigh12 return2 rw weigh15 weigh18 weigh21
        weigh24 weigh27 weigh30 wo x1_0 x1_1 x1_2 x1_3 stat3 turn3 xfront0 xfront1 xback0 xpart0
        xback1 xfin0 xfront2 xpart1 xback2 xfin1 xfront3 xpart2 xback3 xpart3 xfin2 xfin3 y xf_0
        xf_1 stat4_0 turn4_0 weigh flag z4_0
        """.split()
    LATE = ["xf_2", "xf_3", "stat4_1", "turn4_1", "z4_1"]
    FFN_STEPS = {f"{s}{u}" for s in ("up", "silu", "prod", "rest", "high", "down") for u in range(NU)}
    F_STEPS = [s for s in BODY if s in FFN_STEPS or s in LATE or s in ("out0", "out1")]
    EARLY = [s for s in BODY if s not in F_STEPS]
    WEIGHED = 3
    assert FFN_STEPS < set(F_STEPS) and len(BODY) == len(set(BODY)) and set(EARLY) < set(FIRST_ORDER)

    uses = []
    for s in EARLY + LATE:
        if s in ("turn1", "turn2", "return2", "wo", "turn3", "y"):
            uses += [(s, c) for c in range(C)]
        elif s.startswith("turn4"):
            uses += [(s, j) for j in range(C // 2)]
        elif s[:2] == "kv":
            uses += [("k", int(s[2:])), ("v", int(s[2:]))]
        elif s in [f"r{c}" for c in range(C)]:
            uses.append(("r", int(s[1:])))
    USES = len(uses)
    assert C == TB == NB and USES % NB == 0

    def use(s, c):
        return uses.index((s, c))

    ctx = ExitStack()
    with ctx:
        def sb(name, *shape, dt=F32):
            return ctx.enter_context(nc.sbuf_tensor("t_" + name, [P, *shape], dt))

        wk, wv, wr, wo = (sb(n, C, D) for n in ("wk", "wv", "wr", "wo"))
        gate, up = sb("gate", C, I, dt=F32R), sb("up", C, I, dt=F32R)
        down = sb("down", NI, D, dt=F32R)
        vecs = sb("vecs", N_VEC, C)
        fsc = sb("fsc", 2, NI)
        dsb = sb("dsb", D)
        ident = sb("ident", P)
        ramp = sb("ramp", T)
        mhalf = sb("mhalf", TB)
        den_bias = sb("den_bias", 1)
        ew, nw = sb("ew", C), sb("nw", C)
        half_g, half_b = sb("half_g", C), sb("half_b", C)
        rest_tm = sb("rest_tm", 3, C)
        neg_first = sb("neg_first", C)
        neg_wp, bonus = sb("neg_wp", C), sb("bonus", C)
        keep, s_old, c_new = sb("keep", C), sb("s_old", C), sb("c_new", C)
        xres = sb("xres", TB, D)
        xf = sb("xf", TB, D)
        z = sb("z", TB, D)
        zt = sb("zt", C, T)
        mixk = sb("mixk", C, T)
        mixv = sb("mixv", C, T)
        tanh_r = sb("tanh_r", C, T)
        z4h, z4l = sb("z4h", C, T, dt=F32R), sb("z4l", C, T, dt=F32R)
        slot = sb("slot", 2, 4, T)
        pmax = sb("pmax", T + 1)
        gap = sb("gap", T)
        inp = sb("inp", T)
        num_st, den_st = sb("num_st", T + 1), sb("den_st", T + 1)
        silu, h = sb("silu", 2, HALF), sb("h", 3, HALF)
        hh, hl = sb("hh", 3, HALF, dt=F32R), sb("hl", 3, HALF, dt=F32R)
        inexact = sb("inexact", 1)
        ones = sb("ones", 1)
        general = sb("general", 1, dt=I32)
        otile = sb("otile", 2, D)
        stats = sb("stats", TB, 6)
        mv = sb("mv", TB, 2)
        veps, rstd, nmr = sb("veps", TB), sb("rstd", TB), sb("nmr", TB)
        scrap = sb("scrap", 2)
        low_bits = otile[:, :, :].bitcast(I32)
        ctxt = mixv
        wkv = zt

        bank = [ctx.enter_context(nc.psum_tensor(f"bank{j}", [P, T], F32)) for j in range(NB)]
        gu = [ctx.enter_context(nc.psum_tensor(f"gu{j}", [P, 2, HALF], F32)) for j in range(2)]
        dacc = [ctx.enter_context(nc.psum_tensor(f"dacc{j}", [P, D], F32)) for j in range(HB)]

        per, head = {}, {}

        def sem(name, count, before=0):
            s = ctx.enter_context(nc.semaphore(name))
            per[s.name], head[s.name] = count, before
            return s

        x_in, ctx_in = [sem(f"x_in{j}", 16) for j in range(2)], sem("ctx_in", 16)
        filled = sem("filled", USES)
        stat_done, aggr_done = sem("stat_done", 4 * TB), sem("aggr_done", 4 * TB)
        veps_done, rstd_done = sem("veps_done", 8), sem("rstd_done", 8)
        nmr_done = sem("nmr_done", 8)
        z_done, za_done = sem("z_done", 4 * TB // 2), sem("za_done", 4 * TB // 2)
        zt_done = sem("zt_done", C)
        share_done, mix_done = sem("share_done", 3 * C), sem("mix_done", 3 * C)
        tanh_done = sem("tanh_done", C)
        pmax_done, gap_done = sem("pmax_done", C), sem("gap_done", C)
        newv_done = sem("newv_done", C)
        arg_done, relu_done, exp_done = sem("arg_done", 2 * C), sem("relu_done", 2 * C), sem("exp_done", 4 * C)
        ks_done, xexp_done = sem("ks_done", C), sem("xexp_done", 2 * C)
        one_done = sem("one_done", C)
        inp_done = sem("inp_done", 2 * C)
        scan_done = sem("scan_done", 4 * C)
        part_done = sem("part_done", 3 * C)
        num_done, den_done = sem("num_done", 2 * C), sem("den_done", 2 * C)
        log_done, rec_done = sem("log_done", 2 * C), sem("rec_done", 2 * C)
        refine_done = sem("refine_done", 4 * C)
        wkv_done = sem("wkv_done", 2 * C)
        lnt_done, rw_done = sem("lnt_done", C), sem("rw_done", C)
        x1_done, xf_done = sem("x1_done", TB), sem("xf_done", TB)
        z4h_done, z4l_done = sem("z4h_done", C), sem("z4l_done", C)
        hh_done, hl_done = sem("hh_done", NU), sem("hl_done", NU)
        gu_filled = [sem(f"gu_filled{j}", NU // 2) for j in range(2)]
        silu_done, h_done, downed = sem("silu_done", NU), sem("h_done", NU), sem("downed", NU)
        oscaled = sem("oscaled", TB)
        o_done = sem("o_done", TB)
        stored = [sem(f"stored{j}", 16 * TB // 2, 16) for j in range(2)]
        vec_in = sem("vec_in", 0)
        raw_in = {n: sem(f"{n}_raw", 0) for n in ("gate", "up", "down")}
        bits_done, inexact_done, summed, general_done = (
            sem("bits_done", 0), sem("inexact_done", 0), sem("summed", 0), sem("general_done", 0))
        w_in = {n: sem(f"{n}_in", 0) for n in ("wr", "wk", "wv", "wo", "gate", "up", "down")}
        ident_done, const_done, pre_act, pre_dve = (
            sem("ident_done", 0), sem("const_done", 0), sem("pre_act", 0), sem("pre_dve", 0))

        def need(eng, s, b, k):
            v = b * per[s.name] + k + head[s.name]
            if isinstance(v, int) and v <= 0:
                return
            eng.wait_ge(s, v)

        def need_filled(eng, b, s, c):
            need(eng, filled, b, use(s, c) + 1)

        def half(k):
            return slice(k % 2 * HB, (k % 2 + 1) * HB)

        def halves(s, j):
            return bank[use(s, j) % NB][:, :].rearrange("p (c t) -> p c t", c=2)

        READ = {"turn1": zt_done, "r": tanh_done, "k": gap_done, "v": newv_done, "turn2": (z_done, za_done),
                "return2": lnt_done, "wo": x1_done, "turn3": ks_done, "y": xf_done,
                "turn4_0": z4l_done, "turn4_1": z4l_done}

        def need_drained(eng, b, s, c):
            n = use(s, c)
            before, k = uses[n - NB]
            if before == "turn4_1":
                k += C // 2
            s, k = READ[before], k + 1
            if before == "turn2":
                s, k = s[(k - 1) % 2], TB // 2 + (k + 1) // 2
            need(eng, s, b if n >= NB else b - 1, k)

        def run_first(step):
            for s in FIRST_ORDER:
                step(s, 0, None)

        def run_rest(eng, step):
            with eng.Fori(1, B) as b:
                for s in BODY:
                    if s in LATE:
                        step(s, b - 1, None)
                    else:
                        step(s, b, b - 1)
            for s in F_STEPS:
                if s in LATE:
                    step(s, B - 1, None)
                else:
                    step(s, None, B - 1)

        def run(eng, step):
            run_first(step)
            run_rest(eng, step)

        block = ctx.enter_context(nc.Block())

        @block.sync
        def _(sp):
            sp.dma_start(vecs[:, :, :], vecs_in.rearrange("p (n c) -> p n c", c=C)).then_inc(vec_in, 16)

            def load_x(b, hf):
                need(sp, xf_done, b - 1, (hf + 1) * HB)
                src = x[b, :, :] if isinstance(b, int) else x[bass.ds(b, 1), :, :].rearrange("a t d -> (a t) d")
                sp.dma_start(xres[:, hf * HB:(hf + 1) * HB, :],
                             src[hf * HALF:(hf + 1) * HALF, :].rearrange("(n p) d -> p n d", p=P)).then_inc(x_in[hf], 16)

            def load_ctx(b):
                need_filled(sp, b, "v", C - 1)
                src = ctx_t[b, :, :] if isinstance(b, int) else ctx_t[bass.ds(b, 1), :, :].rearrange("a d t -> (a d) t")
                sp.dma_start(ctxt[:, :, :], src.rearrange("(c p) t -> p c t", p=P)).then_inc(ctx_in, 16)

            load_x(0, 0)
            load_x(0, 1)
            for name, tile, src in (("wk", wk, wk_t), ("wv", wv, wv_t), ("wr", wr, wr_t), ("wo", wo, wo_t)):
                sp.dma_start(tile[:, :, :], src.rearrange("(c p) e -> p c e", p=P)).then_inc(w_in[name], 16)
            sp.dma_start(fsc[:, :, :], ffn_scales.rearrange("p (n i) -> p n i", i=NI)).then_inc(stored[0], 16)
            sp.dma_start(dsb[:, :], down_s.to_broadcast([P, D])).then_inc(stored[1], 16)
            ffn_w = (("gate", gate, gate_t), ("up", up, up_t), ("down", down, down_t))
            raw = {n: nc.dram_tensor(f"{n}_words", src.shape, F32, kind="Internal").ap() for n, _, src in ffn_w}

            def copy_words(name, _, src):
                sp.dma_start(raw[name], src).then_inc(raw_in[name], 16)

            def load_words(name, tile, _):
                sp.wait_ge(raw_in[name], 16)
                sp.dma_start(tile[:, :, :].bitcast(F32), raw[name].rearrange("(c p) i -> p c i", p=P)).then_inc(w_in[name], 16)

            copy_words(*ffn_w[0])
            for j in range(len(ffn_w)):
                if j + 1 < len(ffn_w):
                    copy_words(*ffn_w[j + 1])
                load_words(*ffn_w[j])

            def step(s, b, f):
                if s in ("xf_2", "xf_3") and not isinstance(b, int):
                    load_x(b + 1, int(s == "xf_3"))
                if s == "back3":
                    load_ctx(b)
                if s.startswith("out"):
                    for j in range(HB):
                        n = int(s[3:]) * HB + j
                        need(sp, o_done, f, n + 1)
                        dst = out[f, :, :] if isinstance(f, int) else out[bass.ds(f, 1), :, :].rearrange("a t d -> (a t) d")
                        sp.dma_start(dst[n * P:(n + 1) * P, :], otile[:, n % 2, :]).then_inc(stored[n % 2], 16)

            run(sp, step)
            for j in range(2):
                need(sp, stored[j], B, 0)

        @block.gpsimd
        def _(pool):
            pool.memset(ident[:, :], 0.0).then_inc(ident_done, 1)
            pool.wait_ge(ident_done, 1)
            pool.affine_select(out=ident[:, :], in_=ident[:, :], compare_op=ALU.not_equal, fill=1.0,
                               base=0, pattern=[[-1, P]], channel_multiplier=1).then_inc(ident_done, 1)
            pool.memset(mhalf[:, :], -0.5).then_inc(ident_done, 1)
            pool.wait_ge(ident_done, 3)

            def step(s, b, f):
                for k in {"stat1_0": (0,), "stat1": (1,), "stat2": (2, 3), "stat3": (4, 5), "stat4_0": (6,), "stat4_1": (7,)}.get(s, ()):
                    need(pool, veps_done, b, k + 1)
                    pool.tensor_tensor(rstd[:, half(k)], veps[:, half(k)], mhalf[:, half(k)], ALU.pow).then_inc(rstd_done, 1)

            run(pool, step)

        @block.tensor
        def _(pe):
            pe.wait_ge(ident_done, 2)

            def need_normalised(b, k):
                need(pe, (z_done, za_done)[k % 2], b, k // 2 + 1)

            def turn(b, s, src, wait):
                for k in range(NB):
                    wait(k)
                    for m in range(NB):
                        if k == 0:
                            need_drained(pe, b, s, m)
                        done = pe.transpose(bank[m][:, k * P:(k + 1) * P], src[:, k, m * P:(m + 1) * P], ident[:, :])
                        if k == NB - 1:
                            done.then_inc(filled, 1)

            def project(b, s, w, c, src):
                need_drained(pe, b, s, c)
                for k in range(C):
                    if c == 0:
                        need(pe, mix_done, b, ("k", "v", "r").index(s) * C + k + 1)
                    last = pe.matmul(bank[use(s, c) % NB][:, :], w[:, k, c * P:(c + 1) * P], src[:, k, :],
                                     start=(k == 0), stop=(k == C - 1))
                last.then_inc(filled, 1)

            def down_unit(u, f, exact):
                hf, i = divmod(u, NI)
                need(pe, hh_done, f, u + 1)
                need(pe, hl_done, f, u + 1)
                if i == 0 and hf:
                    need(pe, oscaled, f, hf * HB)
                for j in range(HB):
                    for part in (hh, hl):
                        last = pe.matmul(dacc[j][:, :], as_read(part[:, u % 3, j * P:(j + 1) * P], exact),
                                         as_read(down[:, i, :], exact), start=(i == 0 and part is hh),
                                         stop=(i == NI - 1 and part is hl))
                last.then_inc(downed, 1)

            def as_read(ap, exact):
                return ap if exact else ap.bitcast(F32)

            def step(s, b, f):
                first = isinstance(b, int) and b == 0
                if s in ("turn1", "turn3"):
                    turn(b, s, z, lambda k: need_normalised(b, 2 * TB * (s == "turn3") + k))
                elif s.startswith("turn4"):
                    hf = int(s[-1])
                    for k in range(HB):
                        need_normalised(b, 3 * TB + hf * HB + k)
                        for m in range(C):
                            if k == 0 and m % 2 == 0:
                                need_drained(pe, b, s, m // 2)
                            to = halves(s, m // 2)[:, m % 2, k * P:(k + 1) * P]
                            done = pe.transpose(to, z[:, hf * HB + k, m * P:(m + 1) * P], ident[:, :])
                            if k == HB - 1 and m % 2:
                                done.then_inc(filled, 1)
                elif s.startswith("r") and s[1:].isdigit():
                    c = int(s[1:])
                    if first and c == 0:
                        pe.wait_ge(w_in["wr"], 16)
                    project(b, "r", wr, c, z)
                elif s.startswith("kv"):
                    c = int(s[2:])
                    if first and c == 0:
                        pe.wait_ge(w_in["wk"], 16)
                    project(b, "k", wk, c, mixk)
                    if first and c == 0:
                        pe.wait_ge(w_in["wv"], 16)
                    project(b, "v", wv, c, mixv)
                elif s == "turn2":
                    turn(b, s, wkv, lambda k: need(pe, wkv_done, b, k + 1))
                elif s == "return2":
                    turn(b, s, z, lambda k: need_normalised(b, TB + k))
                elif s == "wo":
                    if first:
                        pe.wait_ge(w_in["wo"], 16)
                    for blocks in ((0, 1), *((m,) for m in range(2, TB))):
                        for k in range(C):
                            need(pe, rw_done, b, k + 1)
                            for m in blocks:
                                if k == 0:
                                    need_drained(pe, b, s, m)
                                done = pe.matmul(bank[m][:, :], mixk[:, k, m * P:(m + 1) * P], wo[:, k, :],
                                                 start=(k == 0), stop=(k == C - 1))
                                if k == C - 1:
                                    done.then_inc(filled, 1)
                elif s == "y":
                    turn(b, s, wkv, lambda k: need(pe, wkv_done, b, C + k + 1))
                elif s == "flag":
                    pe.wait_ge(inexact_done, 1)
                    pe.matmul(gu[0][0:1, 0, 0:1], inexact[:, :], ones[:, :], start=True, stop=True).then_inc(summed, 1)

            def ffn_step(s, f, exact):
                if s.startswith("up"):
                    u = int(s[2:])
                    hf, i = divmod(u, NI)
                    if i == 0:
                        need(pe, z4h_done, f, (hf + 1) * C // 2)
                        need(pe, z4l_done, f, (hf + 1) * C // 2)
                    if u >= 2:
                        need(pe, h_done, f, u - 1)
                    for side, w in enumerate((gate, up)):
                        for k in range(C):
                            for part in (z4h, z4l):
                                last = pe.matmul(gu[u % 2][:, side, :], as_read(w[:, k, i * P:(i + 1) * P], exact),
                                                 as_read(part[:, k, hf * HALF:(hf + 1) * HALF], exact),
                                                 start=(k == 0 and part is z4h), stop=(k == C - 1 and part is z4l))
                    last.then_inc(gu_filled[u % 2], 1)
                elif s.startswith("down"):
                    down_unit(int(s[4:]), f, exact)

            run_first(step)
            pe.wait_ge(general_done, 1)
            needs_general = pe.value_load(general[0:1, 0:1], min_val=0, max_val=1)
            with pe.If(needs_general == 0):
                run_rest(pe, lambda s, b, f: (b is not None and step(s, b, f), f is not None and ffn_step(s, f, True)))
            with pe.Else():
                run_rest(pe, lambda s, b, f: (b is not None and step(s, b, f), f is not None and ffn_step(s, f, False)))

        @block.scalar
        def _(act):
            loaded = []

            def table(name):
                if loaded[-1:] != [name]:
                    act.preload_act_table_set(name)
                    loaded.append(name)

            table(EXP_SET)
            act.wait_ge(vec_in, 16)
            act.wait_ge(pre_dve, 1)
            act.activation(ew[:, :], ew[:, :], ACT.Exp).then_inc(pre_act, 1)
            act.activation(keep[:, :], keep[:, :], ACT.Exp).then_inc(pre_act, 1)
            act.activation(s_old[:, :], s_old[:, :], ACT.Exp, scale=-1.0).then_inc(pre_act, 1)

            def split_h(u, f):
                need(act, h_done, f, u + 1)
                if u >= 3:
                    need(act, downed, f, u - 2)
                act.activation(hh[:, u % 3, :], h[:, u % 3, :], ACT.Copy).then_inc(hh_done, 1)

            def normalise(b, k, src):
                need(act, nmr_done, b, k + 1)
                t = k % 2 * HB + 1
                act.activation(z[:, t, :], src(t), ACT.Identity, scale=rstd[:, t:t + 1],
                               bias=nmr[:, t:t + 1]).then_inc(za_done, 1)

            def share(tm, dst, c, src):
                act.activation(dst[:, c, :], src, ACT.Copy, scale=vecs[:, tm, c:c + 1]).then_inc(share_done, 1)

            def step(s, b, f):
                if s == BODY[0]:
                    loaded.clear()
                if s == "stat1":
                    need_filled(act, b - 1, "turn4_1", C // 2 - 1)
                    normalise(b, 0, lambda t: xres[:, t, :])
                    normalise(b, 1, lambda t: xres[:, t, :])
                elif s == "stat3":
                    normalise(b, 4, lambda t: xres[:, t, :])
                    normalise(b, 5, lambda t: xres[:, t, :])
                elif s.startswith("stat4"):
                    normalise(b, 6 + int(s[-1]), lambda t: xf[:, t, :])
                elif s == "turn1":
                    for c in range(C):
                        need_filled(act, b, s, c)
                        share(TM_K, mixk, c, bank[c][:, :])
                        act.activation(zt[:, c, :], bank[c][:, :], ACT.Copy).then_inc(zt_done, 1)
                    for c in range(C):
                        need(act, zt_done, b, c + 1)
                        share(TM_V, mixv, c, zt[:, c, :])
                elif s == "mix_r":
                    for c in range(C):
                        share(TM_R, z, c, zt[:, c, :])
                elif s.startswith("tanh"):
                    c = int(s[4:])
                    table(SILU_SET)
                    need_filled(act, b, "r", c)
                    act.activation(tanh_r[:, c, :], bank[use("r", c) % NB][:, :], ACT.Tanh, scale=0.5).then_inc(tanh_done, 1)
                elif s.startswith("front"):
                    c = int(s[5:])
                    table(EXP_SET)
                    sl = slot[:, c % 2]
                    need(act, gap_done, b, c + 1)
                    act.activation(sl[:, 3, :], gap[:, :], ACT.Relu, bias=neg_first[:, c:c + 1]).then_inc(relu_done, 1)
                    need(act, arg_done, b, 2 * c + 1)
                    act.activation(sl[:, 0, :], sl[:, 0, :], ACT.Exp, scale=-1.0).then_inc(exp_done, 1)
                    act.activation(sl[:, 2, :], gap[:, :], ACT.Relu, bias=vecs[:, FIRST, c:c + 1], scale=-1.0).then_inc(relu_done, 1)
                    need(act, arg_done, b, 2 * c + 2)
                    act.activation(sl[:, 1, :], sl[:, 1, :], ACT.Exp).then_inc(exp_done, 1)
                    need(act, relu_done, b, 2 * c + 2)
                    act.activation(sl[:, 3, :], sl[:, 3, :], ACT.Exp, scale=-1.0).then_inc(exp_done, 1)
                    act.activation(sl[:, 2, :], sl[:, 2, :], ACT.Exp, scale=-1.0).then_inc(exp_done, 1)
                elif s.startswith("part"):
                    c = int(s[4:])
                    table(EXP_SET)
                    need(act, den_done, b, c + 1)
                    act.activation(slot[:, c % 2, 1, :], slot[:, c % 2, 0, :], ACT.Ln, scale=2.0 ** -DEN_SHIFT).then_inc(log_done, 1)
                    need(act, log_done, b, c + 1)
                    act.activation(slot[:, c % 2, 1, :], slot[:, c % 2, 1, :], ACT.Exp, scale=-1.0,
                                   bias=den_bias[:, :]).then_inc(rec_done, 1)
                elif s == "stat2":
                    need_filled(act, b, "turn2", TB - 1)
                    normalise(b, 2, lambda t: bank[t][:, :])
                    normalise(b, 3, lambda t: bank[t][:, :])
                elif s == "rw":
                    for c in range(C):
                        need_filled(act, b, "return2", c)
                        act.activation(mixk[:, c, :], bank[c][:, :], ACT.Identity, scale=half_g[:, c:c + 1],
                                       bias=half_b[:, c:c + 1]).then_inc(lnt_done, 1)
                elif s.startswith("xfront"):
                    c = int(s[6:])
                    table(EXP_SET)
                    need(act, ks_done, b, c + 1)
                    act.activation(slot[:, c % 2, 1, 1:], slot[:, c % 2, 0, 1:], ACT.Exp, bias=c_new[:, c:c + 1]).then_inc(xexp_done, 1)
                    act.activation(slot[:, c % 2, 3, :], slot[:, c % 2, 0, :], ACT.Exp).then_inc(xexp_done, 1)
                elif s.startswith("xpart"):
                    c = int(s[5:])
                    table(EXP_SET)
                    need(act, den_done, b, C + c + 1)
                    act.activation(slot[:, c % 2, 1, :], slot[:, c % 2, 3, :], ACT.Ln).then_inc(log_done, 1)
                    need(act, log_done, b, C + c + 1)
                    act.activation(slot[:, c % 2, 1, :], slot[:, c % 2, 1, :], ACT.Exp, scale=-1.0).then_inc(rec_done, 1)
                elif s.startswith("z4"):
                    hf = int(s[-1])
                    tokens = slice(hf * HALF, (hf + 1) * HALF)
                    for j in range(C // 2):
                        need_filled(act, b, f"turn4_{hf}", j)
                        act.activation(z4h[:, 2 * j:2 * j + 2, tokens], halves(f"turn4_{hf}", j), ACT.Copy).then_inc(z4h_done, 1)
                elif s.startswith("silu"):
                    u = int(s[4:])
                    table(SILU_SET)
                    need(act, gu_filled[u % 2], f, u // 2 + 1)
                    act.activation(silu[:, u % 2, :], gu[u % 2][:, 0, :], ACT.Silu,
                                   scale=fsc[:, 0, u % NI:u % NI + 1]).then_inc(silu_done, 1)
                elif s.startswith("high"):
                    split_h(int(s[4:]), f)
                elif s == "flag":
                    act.wait_ge(stored[0], 16)

            run(act, step)

        @block.vector
        def _(dve):
            dve.memset(pmax[:, 0:1], -1e38)
            dve.memset(num_st[:, 0:1], 0.0)
            dve.memset(den_st[:, 0:1], 0.0)
            dve.memset(scrap[:, :], 0.0)
            dve.memset(ones[:, :], 1.0)
            dve.memset(gap[:, :], 1.0)
            dve.memset(den_bias[:, :], -DEN_SHIFT * LN2).then_inc(const_done, 1)
            dve.wait_ge(const_done, 1)
            dve.tensor_tensor_scan(ramp[:, :], gap[:, :], gap[:, :], -1.0, ALU.add, ALU.mult).then_inc(const_done, 1)
            dve.wait_ge(vec_in, 16)
            dve.tensor_scalar(neg_wp[:, :], vecs[:, XW, :], 0.0, -1.0, ALU.max, ALU.mult).then_inc(const_done, 1)
            dve.tensor_scalar(keep[:, :], vecs[:, XW, :], 0.0, None, ALU.min).then_inc(const_done, 1)
            dve.wait_ge(const_done, 4)
            dve.tensor_tensor(bonus[:, :], vecs[:, XU, :], neg_wp[:, :], ALU.subtract).then_inc(const_done, 1)
            dve.wait_ge(const_done, 5)
            dve.tensor_scalar(ew[:, :], vecs[:, DECAY, :], 88.0, None, ALU.min)
            dve.tensor_scalar(c_new[:, :], bonus[:, :], 0.0, None, ALU.min)
            dve.tensor_scalar(half_g[:, :], vecs[:, LN_G, :], 0.5, None, ALU.mult)
            dve.tensor_scalar(rest_tm[:, :, :], vecs[:, TM_K:TM_R + 1, :], -1.0, 1.0, ALU.mult, ALU.add)
            dve.tensor_scalar(neg_first[:, :], vecs[:, FIRST, :], -1.0, None, ALU.mult)
            dve.tensor_scalar(half_b[:, :], vecs[:, LN_B, :], 0.5, None, ALU.mult)
            dve.tensor_scalar(s_old[:, :], bonus[:, :], 0.0, None, ALU.max).then_inc(pre_dve, 1)
            dve.wait_ge(pre_act, 3)
            dve.tensor_scalar(nw[:, :], ew[:, :], -1.0, None, ALU.mult).then_inc(const_done, 1)
            dve.wait_ge(const_done, 6)

            def token_stats(t, tile):
                dve.bn_stats(stats[:, t, :], tile).then_inc(stat_done, 1)

            def measure(b, k):
                need(dve, stat_done, b, (k + 1) * HB)
                dve.memset(scrap[:, 0:1], 0.0)
                for t in range(TB)[half(k)]:
                    dve.bn_aggr(mv[:, t, :], stats[:, t, :]).then_inc(aggr_done, 1)
                need(dve, aggr_done, b, (k + 1) * HB)
                need(dve, za_done, b, k - 1)
                dve.tensor_scalar(veps[:, half(k)], mv[:, half(k), 1], EPS, None, ALU.add).then_inc(veps_done, 1)

            def normalise(b, k, src):
                need(dve, rstd_done, b, k + 1)
                dve.scalar_tensor_tensor(out=nmr[:, half(k)], in0=mv[:, half(k), 0], scalar=-1.0, in1=rstd[:, half(k)],
                                         op0=ALU.mult, op1=ALU.mult).then_inc(nmr_done, 1)
                t = k % 2 * HB
                dve.tensor_scalar(z[:, t, :], src(t), mv[:, t, 0:1], rstd[:, t:t + 1],
                                  ALU.subtract, ALU.mult).then_inc(z_done, 1)

            def refine(b, c, r, num, den):
                sl = slot[:, c % 2]
                need(dve, rec_done, b, r + 1)
                dve.tensor_tensor(sl[:, den, :], sl[:, den, :], sl[:, 1, :], ALU.mult).then_inc(refine_done, 1)
                dve.tensor_tensor(sl[:, num, :], sl[:, num, :], sl[:, 1, :], ALU.mult).then_inc(refine_done, 1)
                need(dve, refine_done, b, 2 * r + 2)
                dve.scalar_tensor_tensor(out=wkv[:, c, :], in0=sl[:, den, :], scalar=2.0, in1=sl[:, num, :],
                                         op0=ALU.subtract, op1=ALU.mult, reverse0=True).then_inc(wkv_done, 1)

            def mix(b, tm, dst):
                for c in range(C):
                    need(dve, zt_done, b, c + 1)
                    need(dve, share_done, b, (tm - TM_K) * C + c + 1)
                    dve.scalar_tensor_tensor(out=dst[:, c, 1:], in0=zt[:, c, 0:T - 1], scalar=rest_tm[:, tm - TM_K, c:c + 1],
                                             in1=dst[:, c, 1:], op0=ALU.mult, op1=ALU.add).then_inc(mix_done, 1)

            def rest_h(u, f):
                need(dve, hh_done, f, u + 1)
                dve.tensor_tensor(hl[:, u % 3, :], h[:, u % 3, :], hh[:, u % 3, :].bitcast(F32),
                                  ALU.subtract).then_inc(hl_done, 1)

            def step(s, b, f):
                if s in ("stat1_0", "stat1"):
                    k = int(s == "stat1")
                    need(dve, x_in[k], b, 16)
                    for t in range(TB)[half(k)]:
                        token_stats(t, xres[:, t, :])
                    measure(b, k)
                    if k:
                        need_filled(dve, b - 1, "turn4_1", C // 2 - 1)
                        normalise(b, 0, lambda t: xres[:, t, :])
                        normalise(b, 1, lambda t: xres[:, t, :])
                elif s == "mix_k":
                    mix(b, TM_K, mixk)
                elif s == "mix_v":
                    mix(b, TM_V, mixv)
                elif s == "mix_r":
                    mix(b, TM_R, z)
                elif s.startswith("front"):
                    c = int(s[5:])
                    sl = slot[:, c % 2]
                    kb = bank[use("k", c) % NB]
                    need_filled(dve, b, "k", c)
                    dve.tensor_tensor_scan(pmax[:, 1:], nw[:, c:c + 1].to_broadcast([P, T]), kb[:, :], -1e38,
                                           ALU.add, ALU.max).then_inc(pmax_done, 1)
                    need(dve, pmax_done, b, c + 1)
                    dve.tensor_tensor(gap[:, :], pmax[:, 0:T], kb[:, :], ALU.subtract).then_inc(gap_done, 1)
                    need(dve, gap_done, b, c + 1)
                    dve.tensor_scalar(sl[:, 0, :], gap[:, :], nw[:, c:c + 1], 0.0, ALU.add, ALU.max).then_inc(arg_done, 1)
                    dve.tensor_scalar(sl[:, 1, :], gap[:, :], ew[:, c:c + 1], None, ALU.min).then_inc(arg_done, 1)
                elif s.startswith("back"):
                    c = int(s[4:])
                    sl = slot[:, c % 2]
                    vb = bank[use("v", c) % NB]
                    need_filled(dve, b, "v", c)
                    need(dve, exp_done, b, 4 * c + 1)
                    dve.tensor_tensor(inp[:, :], sl[:, 0, :], vb[:, :], ALU.mult).then_inc(inp_done, 1)
                    need(dve, exp_done, b, 4 * c + 2)
                    need(dve, den_done, b, c)
                    dve.tensor_tensor_scan(den_st[:, 1:], sl[:, 1, :], sl[:, 0, :], 0.0, ALU.mult, ALU.add).then_inc(scan_done, 1)
                    need(dve, num_done, b, c)
                    need(dve, inp_done, b, c + 1)
                    dve.tensor_tensor_scan(num_st[:, 1:], sl[:, 1, :], inp[:, :], 0.0, ALU.mult, ALU.add).then_inc(scan_done, 1)
                    need(dve, exp_done, b, 4 * c + 3)
                    dve.tensor_tensor(gap[:, :], sl[:, 3, :], vb[:, :], ALU.mult).then_inc(newv_done, 1)
                elif s.startswith("part"):
                    c = int(s[4:])
                    sl = slot[:, c % 2]
                    need(dve, scan_done, b, 2 * c + 2)
                    need(dve, exp_done, b, 4 * c + 4)
                    dve.tensor_tensor(sl[:, 0, :], sl[:, 2, :], den_st[:, 0:T], ALU.mult).then_inc(part_done, 1)
                    dve.tensor_tensor(sl[:, 2, :], sl[:, 2, :], num_st[:, 0:T], ALU.mult).then_inc(part_done, 1)
                    need(dve, part_done, b, 2 * c + 1)
                    dve.tensor_tensor(sl[:, 0, :], sl[:, 0, :], sl[:, 3, :], ALU.add).then_inc(den_done, 1)
                    need(dve, part_done, b, 2 * c + 2)
                    need(dve, newv_done, b, c + 1)
                    dve.tensor_tensor(sl[:, 2, :], sl[:, 2, :], gap[:, :], ALU.add).then_inc(num_done, 1)
                elif s.startswith("fin"):
                    c = int(s[3:])
                    need(dve, num_done, b, c + 1)
                    refine(b, c, c, 2, 0)
                elif s == "stat2":
                    for t in range(TB):
                        need_filled(dve, b, "turn2", t)
                        token_stats(t, bank[t][:, :])
                        if t == HB - 1:
                            measure(b, 2)
                    measure(b, 3)
                    normalise(b, 2, lambda t: bank[t][:, :])
                    normalise(b, 3, lambda t: bank[t][:, :])
                elif s == "rw":
                    for c in range(C):
                        need(dve, lnt_done, b, c + 1)
                        dve.scalar_tensor_tensor(out=mixk[:, c, :], in0=tanh_r[:, c, :], scalar=1.0, in1=mixk[:, c, :],
                                                 op0=ALU.add, op1=ALU.mult).then_inc(rw_done, 1)
                elif s.startswith("x1_"):
                    t = int(s[3:])
                    need_filled(dve, b, "wo", t)
                    dve.tensor_tensor(xres[:, t, :], bank[t][:, :], xres[:, t, :], ALU.add).then_inc(x1_done, 1)
                    need(dve, x1_done, b, t + 1)
                    token_stats(t, xres[:, t, :])
                    if t % HB == HB - 1:
                        measure(b, 4 + t // HB)
                elif s == "stat3":
                    normalise(b, 4, lambda t: xres[:, t, :])
                    normalise(b, 5, lambda t: xres[:, t, :])
                elif s.startswith("xfront"):
                    c = int(s[6:])
                    need_filled(dve, b, "turn3", c)
                    dve.memset(slot[:, c % 2, 1, 0:1], 1.0).then_inc(one_done, 1)
                    dve.scalar_tensor_tensor(out=slot[:, c % 2, 0, :], in0=ramp[:, :], scalar=neg_wp[:, c:c + 1],
                                             in1=bank[c][:, :], op0=ALU.mult, op1=ALU.add).then_inc(ks_done, 1)
                elif s.startswith("xback"):
                    c = int(s[5:])
                    sl = slot[:, c % 2]
                    if c == 0:
                        need(dve, ctx_in, b, 16)
                    v = ctxt[:, c, :]
                    decay = keep[:, c:c + 1].to_broadcast([P, T])
                    need(dve, xexp_done, b, 2 * c + 2)
                    dve.tensor_tensor(inp[:, :], sl[:, 3, :], v, ALU.mult).then_inc(inp_done, 1)
                    need(dve, den_done, b, C + c)
                    dve.tensor_tensor_scan(den_st[:, 1:], decay, sl[:, 3, :], 0.0, ALU.mult, ALU.add).then_inc(scan_done, 1)
                    need(dve, num_done, b, C + c)
                    need(dve, inp_done, b, C + c + 1)
                    dve.tensor_tensor_scan(num_st[:, 1:], decay, inp[:, :], 0.0, ALU.mult, ALU.add).then_inc(scan_done, 1)
                    need(dve, one_done, b, c + 1)
                    dve.tensor_tensor(sl[:, 2, :], sl[:, 1, :], v, ALU.mult).then_inc(part_done, 1)
                elif s.startswith("xpart"):
                    c = int(s[5:])
                    sl = slot[:, c % 2]
                    need(dve, scan_done, b, 2 * C + 2 * c + 2)
                    dve.scalar_tensor_tensor(out=sl[:, 3, :], in0=den_st[:, 0:T], scalar=s_old[:, c:c + 1],
                                             in1=sl[:, 1, :], op0=ALU.mult, op1=ALU.add).then_inc(den_done, 1)
                    need(dve, part_done, b, 2 * C + c + 1)
                    dve.scalar_tensor_tensor(out=sl[:, 2, :], in0=num_st[:, 0:T], scalar=s_old[:, c:c + 1],
                                             in1=sl[:, 2, :], op0=ALU.mult, op1=ALU.add).then_inc(num_done, 1)
                elif s.startswith("xfin"):
                    c = int(s[4:])
                    need(dve, num_done, b, C + c + 1)
                    refine(b, c, C + c, 2, 3)
                elif s.startswith("xf_"):
                    t = int(s[3:])
                    if f is not None:
                        need(dve, o_done, f, t + 1)
                    need_filled(dve, b, "y", t)
                    dve.tensor_tensor(xf[:, t, :], bank[t][:, :], xres[:, t, :], ALU.add).then_inc(xf_done, 1)
                    need(dve, xf_done, b, t + 1)
                    token_stats(t, xf[:, t, :])
                    if t % HB == HB - 1:
                        measure(b, 6 + t // HB)
                elif s.startswith("stat4"):
                    normalise(b, 6 + int(s[-1]), lambda t: xf[:, t, :])
                elif s.startswith("z4"):
                    hf = int(s[-1])
                    tokens = slice(hf * HALF, (hf + 1) * HALF)
                    for j in range(C // 2):
                        need(dve, z4h_done, b, hf * C // 2 + j + 1)
                        part = z4h[:, 2 * j:2 * j + 2, tokens].bitcast(F32)
                        dve.tensor_tensor(z4l[:, 2 * j:2 * j + 2, tokens], halves(f"turn4_{hf}", j), part,
                                          ALU.subtract).then_inc(z4l_done, 1)
                elif s.startswith("prod"):
                    u = int(s[4:])
                    need(dve, silu_done, f, u + 1)
                    if u >= 3:
                        need(dve, hl_done, f, u - 2)
                    dve.scalar_tensor_tensor(out=h[:, u % 3, :], in0=gu[u % 2][:, 1, :],
                                             scalar=fsc[:, 1, u % NI:u % NI + 1], in1=silu[:, u % 2, :],
                                             op0=ALU.mult, op1=ALU.mult).then_inc(h_done, 1)
                elif s.startswith("rest"):
                    rest_h(int(s[4:]), f)
                elif s.startswith("weigh") and s[5:]:
                    for n in range(int(s[5:]), int(s[5:]) + WEIGHED):
                        name, tile = (("gate", gate), ("up", up), ("down", down))[n // NI]
                        if n % NI == 0:
                            dve.wait_ge(w_in[name], 16)
                        k = n % NI * D
                        words = tile[:, :, :].bitcast(I32).rearrange("p a b -> p (a b)")[:, k:k + D]
                        if n < 2:
                            dve.tensor_scalar(low_bits[:, n % 2, :], words, F32R_LOST, None,
                                              ALU.bitwise_and).then_inc(bits_done, 1)
                        else:
                            dve.wait_ge(bits_done, n - 1)
                            dve.tensor_tensor(low_bits[:, n % 2, :], low_bits[:, n % 2, :], words,
                                              ALU.bitwise_or).then_inc(bits_done, 1)
                elif s == "weigh":
                    n = 3 * NI
                    dve.wait_ge(bits_done, n)
                    dve.tensor_tensor(low_bits[:, 0, :], low_bits[:, 0, :], low_bits[:, 1, :],
                                      ALU.bitwise_or).then_inc(bits_done, 1)
                    dve.wait_ge(bits_done, n + 1)
                    dve.tensor_scalar(low_bits[:, 0, :], low_bits[:, 0, :], F32R_LOST, None,
                                      ALU.bitwise_and).then_inc(bits_done, 1)
                    dve.wait_ge(bits_done, n + 2)
                    dve.reduce_max(inexact[:, :], low_bits[:, 0, :], AXIS_X).then_inc(inexact_done, 1)
                elif s == "flag":
                    dve.wait_ge(stored[0], 16)
                    dve.wait_ge(stored[1], 16)
                    dve.wait_ge(summed, 1)
                    dve.tensor_scalar(general[0:1, :], gu[0][0:1, 0, 0:1], 0.0, None, ALU.is_gt).then_inc(general_done, 1)
                elif s.startswith("out"):
                    hf = int(s[3:])
                    need(dve, downed, f, (hf + 1) * NI)
                    for j in range(HB):
                        n = hf * HB + j
                        need(dve, stored[n % 2], f, 16 * (n // 2))
                        dve.tensor_tensor(otile[:, n % 2, :], dacc[j][:, :], dsb[:, :], ALU.mult).then_inc(oscaled, 1)
                        need(dve, oscaled, f, n + 1)
                        dve.tensor_tensor(otile[:, n % 2, :], otile[:, n % 2, :], xf[:, n, :], ALU.add).then_inc(o_done, 1)

            run(dve, step)


def kernel(**inputs):
    import numpy as _np
    import concourse.bacc as _bacc
    from concourse import mybir as _mybir
    from concourse.bass_utils import run_bass_kernel_spmd as _run

    def columns(v):
        return _np.asarray(v).reshape(-1, P).T

    def turned(w):
        return _np.ascontiguousarray(_np.asarray(w).T)

    arrays = {
        "x": _np.ascontiguousarray(inputs["x"]),
        "ctx_t": _np.ascontiguousarray(_np.asarray(inputs["ctx_2048"]).transpose(0, 2, 1)),
        "wk_t": turned(inputs["L0_attn_Wk"]),
        "wv_t": turned(inputs["L0_attn_Wv"]),
        "wr_t": turned(inputs["L0_attn_Wr"]),
        "wo_t": turned(inputs["L0_attn_Wo"]),
        "vecs": _np.ascontiguousarray(_np.concatenate([columns(inputs[n]) for n in (
            "L0_attn_tm_k", "L0_attn_tm_v", "L0_attn_tm_r", "L0_attn_time_decay", "L0_attn_time_first",
            "L0_attn_ln_g", "L0_attn_ln_b", "L0_xattn_w", "L0_xattn_u")], axis=1)),
        "gate_t": turned(inputs["L0_ffn_gate_w"]),
        "up_t": turned(inputs["L0_ffn_up_w"]),
        "down_t": turned(inputs["L0_ffn_down_w"]),
        "ffn_scales": _np.ascontiguousarray(_np.concatenate(
            [columns(inputs["L0_ffn_gate_s"]), columns(inputs["L0_ffn_up_s"])], axis=1)),
        "down_s": _np.ascontiguousarray(_np.asarray(inputs["L0_ffn_down_s"]).reshape(1, -1)),
    }
    nc = _bacc.Bacc("TRN2", target_bir_lowering=False, num_devices=1, dynamic_dma_scratch_size=1024)
    args = [nc.dram_tensor("in_" + n, a.shape, _mybir.dt.from_np(a.dtype), kind="ExternalInput").ap() for n, a in arrays.items()]
    out = nc.dram_tensor("out", arrays["x"].shape, _mybir.dt.float32, kind="ExternalOutput").ap()
    decoder_layer(nc, *args, out)
    r = _run(nc, [{"in_" + n: a for n, a in arrays.items()}], core_ids=[0])
    return r.results[0]["out"]
```
